# Optimizing a Trainium2 kernel written in Bass

```python
import numpy as np
import jax
import jax.numpy as jnp

def _softmax(x, axis=-1):
    return jax.nn.softmax(x, axis=axis)

def _gelu(x):
    return jax.nn.gelu(x, approximate=True)

def _silu(x):
    return jax.nn.silu(x)

def _sigmoid(x):
    return jax.nn.sigmoid(x)

def _layernorm(x, axis=-1, eps=1e-05):
    m = jnp.mean(x, axis=axis, keepdims=True)
    v = jnp.var(x, axis=axis, keepdims=True)
    return (x - m) / jnp.sqrt(v + eps)

def _scatter_add(tgt, idx, src, axis=0):
    return tgt.at[idx].add(src)

def _segment_sum(src, seg, n):
    return jax.ops.segment_sum(src, seg, n)
kernel_name = 'mk_sandwich_d1_jaxref_r8_bfec11'

def setup_inputs(seed: int=0):
    np.random.seed(seed)
    _w = jnp.asarray

    def _L0_attn_setup():
        import jax, jax.numpy as jnp
        import numpy as np
        H = 8
        D = 64
        E = 128

        def sinusoidal_pe(T, d, dtype=jnp.float32):
            pos = jnp.arange(T, dtype=jnp.float32)[:, None]
            div = jnp.exp(jnp.arange(0, d, 2, dtype=jnp.float32) * (-np.log(10000.0) / d))
            ang = pos * div
            pe = jnp.stack([jnp.sin(ang), jnp.cos(ang)], axis=-1).reshape(T, d)
            return pe.astype(dtype)
        key = jax.random.key(seed)
        k1, k2, k3 = jax.random.split(key, 3)
        B, T = (2, 256)
        x = jax.random.normal(k1, (B, T, E), dtype=jnp.float32)
        Wqkv = jax.random.normal(k2, (3 * H * D, E), dtype=jnp.float32) * (1.0 / np.sqrt(E))
        Wo = jax.random.normal(k3, (E, H * D), dtype=jnp.float32) * (1.0 / np.sqrt(H * D))
        return {'x': x, 'Wqkv': Wqkv, 'Wo': Wo}
    _L0_attn_in = _L0_attn_setup()

    def _L0_ffn_setup():
        import jax, jax.numpy as jnp
        import numpy as np
        D_MODEL = 128
        key = jax.random.key(seed)
        k_x, k_w, k_a1, k_a2 = jax.random.split(key, 4)
        x = jax.random.normal(k_x, (4, 256, D_MODEL), dtype=jnp.float32)
        weight = jax.random.normal(k_w, (D_MODEL, D_MODEL), dtype=jnp.float32) * 0.02
        aux_weight1 = jax.random.normal(k_a1, (D_MODEL, D_MODEL), dtype=jnp.float32) * 0.02
        aux_weight2 = jax.random.normal(k_a2, (D_MODEL, D_MODEL), dtype=jnp.float32) * 0.02
        bias = jnp.zeros((D_MODEL,), dtype=jnp.float32)
        return {'x': x, 'weight': weight, 'aux_weight1': aux_weight1, 'aux_weight2': aux_weight2, 'bias': bias}
    _L0_ffn_in = _L0_ffn_setup()
    _d = {'L0_attn_x': _L0_attn_in['x'], 'L0_attn_Wqkv': _L0_attn_in['Wqkv'], 'L0_attn_Wo': _L0_attn_in['Wo'], 'L0_ffn_weight': _L0_ffn_in['weight'], 'L0_ffn_aux_weight1': _L0_ffn_in['aux_weight1'], 'L0_ffn_aux_weight2': _L0_ffn_in['aux_weight2'], 'L0_ffn_bias': _L0_ffn_in['bias']}
    _x0 = _d['L0_attn_x']
    _d['L0_attn_x'] = jax.random.normal(jax.random.fold_in(jax.random.key(seed), 1), (32, 256, 128), dtype=_x0.dtype)
    del _x0
    return _d

def reference(L0_attn_x, L0_attn_Wqkv, L0_attn_Wo, L0_ffn_weight, L0_ffn_aux_weight1, L0_ffn_aux_weight2, L0_ffn_bias):

    def _L0_attn_ref(x, Wqkv, Wo):
        import jax, jax.numpy as jnp
        import numpy as np
        H = 8
        D = 64
        E = 128

        def sinusoidal_pe(T, d, dtype=jnp.float32):
            pos = jnp.arange(T, dtype=jnp.float32)[:, None]
            div = jnp.exp(jnp.arange(0, d, 2, dtype=jnp.float32) * (-np.log(10000.0) / d))
            ang = pos * div
            pe = jnp.stack([jnp.sin(ang), jnp.cos(ang)], axis=-1).reshape(T, d)
            return pe.astype(dtype)
        B, T, _ = x.shape
        qkv = jnp.einsum('bte,fe->btf', x, Wqkv)
        qkv = qkv.reshape(B, T, H, 3 * D)
        q, k, v = jnp.split(qkv, 3, axis=-1)
        q = q.transpose(0, 2, 1, 3)
        k = k.transpose(0, 2, 1, 3)
        v = v.transpose(0, 2, 1, 3)
        pe = sinusoidal_pe(T, D, q.dtype)
        q = q + pe[None, None]
        k = k + pe[None, None]
        causal = jnp.tril(jnp.ones((T, T), dtype=bool))
        scores = jnp.einsum('bhtd,bhsd->bhts', q, k) / jnp.sqrt(jnp.asarray(D, q.dtype))
        scores = jnp.where(causal[None, None], scores, jnp.asarray(-jnp.inf, q.dtype))
        probs = jax.nn.softmax(scores, axis=-1)
        attn = jnp.einsum('bhts,bhsd->bhtd', probs, v)
        out = attn.transpose(0, 2, 1, 3).reshape(B, T, H * D)
        out = jnp.einsum('btf,ef->bte', out, Wo)
        return out

    def _L0_ffn_ref(x, weight, aux_weight1, aux_weight2, bias):
        import jax, jax.numpy as jnp
        import numpy as np
        D_MODEL = 128
        h = jnp.einsum('btc,cd->btd', x, weight)
        h = jnp.einsum('btc,cd->btd', h, aux_weight1)
        h = jnp.einsum('btc,cd->btd', h, aux_weight2)
        return jnp.tanh(h + bias)
    x = L0_attn_x
    x = x + _layernorm(_L0_attn_ref(_layernorm(x, axis=-1), L0_attn_Wqkv, L0_attn_Wo), axis=-1)
    x = x + _layernorm(_L0_ffn_ref(_layernorm(x, axis=-1), L0_ffn_weight, L0_ffn_aux_weight1, L0_ffn_aux_weight2, L0_ffn_bias), axis=-1)
    return x

_drawn_inputs = setup_inputs


def setup_inputs(seed=0):
    import zlib

    import numpy as np

    out = dict(_drawn_inputs(seed))
    spreads = {'L0_ffn_bias': (0.0, 0.1)}
    factors = {}
    for name, (base, spread) in spreads.items():
        noise = np.random.default_rng([zlib.crc32(name.encode()), seed]).standard_normal(out[name].shape)
        drawn = base * np.exp(spread * noise) if base else spread * noise
        out[name] = jnp.asarray(drawn.astype(out[name].dtype))
    for name, factor in factors.items():
        out[name] = (out[name] * factor).astype(out[name].dtype)
    return out
```

```python
from contextlib import ExitStack

import numpy as np

import concourse.bass as bass
from concourse import mybir

ALU = mybir.AluOpType
ACT = mybir.ActivationFunctionType
AX_X = mybir.AxisListType.X
F32 = mybir.dt.float32
F32R = mybir.dt.float32r
BF16 = mybir.dt.bfloat16

P = 128
EPS = 1e-5
MASKED = -3.0e38


class Batch:

    def __init__(self, half, parity, total):
        self.half, self.parity, self.total = half, parity, total

    def plus(self, n):
        q, parity = divmod(self.parity + n, 2)
        return Batch(self.half + q, parity, self.total)

    def times(self, k, add=0):
        return self.half * (2 * k) + (k * self.parity + add)

    def exists(self):
        return not isinstance(self.half, int) or 0 <= 2 * self.half + self.parity < self.total


def wait(eng, sem, value):
    if not isinstance(value, int) or value > 0:
        eng.wait_ge(sem, value)


def constants(T, D):
    pos = np.arange(T, dtype=np.float32)[:, None]
    div = np.exp(np.arange(0, D, 2, dtype=np.float32) * np.float32(-np.log(10000.0) / D))
    ang = (pos * div.astype(np.float32)).astype(np.float32)
    pe = np.stack([np.sin(ang), np.cos(ang)], axis=-1).reshape(T, D).astype(np.float32)
    pe_t = np.concatenate([pe.T, pe.T], axis=0)
    scale = np.float32(D ** -0.5)
    pe_qk = np.concatenate([pe_t * scale, pe_t], axis=1)
    causal = np.where(np.arange(P)[None, :] <= np.arange(P)[:, None], 0.0, MASKED).astype(np.float32)
    mask = np.concatenate([causal, causal], axis=1)
    return np.ascontiguousarray(pe_qk), np.ascontiguousarray(mask), np.eye(P, dtype=np.float32)


def build_block(nc, x, w_qkv_t, w_o_t, w1_t, w2, w3, bias, out, H):
    B, T, E = x.shape
    D = w_o_t.shape[0] // H
    TT = T // P
    PAIRS = H // 2
    F = H * D
    SCALE = float(D) ** -0.5
    assert E == P and TT == 2 and 2 * D == P and PAIRS == 4 and B % 2 == 0 and B >= 10
    G = B * PAIRS
    SC = T + P

    pe_np, mask_np, ident_np = constants(T, D)
    pe_dram = nc.inline_tensor(pe_np, name="pe_table").ap()
    mask_dram = nc.inline_tensor(mask_np, name="causal_mask").ap()
    ident_dram = nc.inline_tensor(ident_np, name="identity").ap()

    x_dram = x.rearrange("b (t p) e -> p b t e", p=P)
    out_dram = out.rearrange("b (t p) e -> p b t e", p=P)

    with ExitStack() as ctx:
        def sb(name, shape, dt=F32):
            return ctx.enter_context(nc.sbuf_tensor(name, shape, dt))

        def sem(name):
            return ctx.enter_context(nc.semaphore(name))

        s_bank = [[ctx.enter_context(nc.psum_tensor(f"scores_{h}_{i}", [P, 512], F32)) for i in range(2)]
                  for h in range(2)]
        turn_bank = ctx.enter_context(nc.psum_tensor("turned_probs", [P, 2, T], F32))
        turn_out_bank = ctx.enter_context(nc.psum_tensor("turned_probs_and_heads", [P, 512], F32))
        qk_bank = ctx.enter_context(nc.psum_tensor("qk_bank", [P, 512], F32))
        misc_bank = ctx.enter_context(nc.psum_tensor("misc_bank", [P, 512], F32))

        w_raw = sb("w_raw", [P, 3 * F])
        w_hi = sb("w_hi", [P, 3 * F], F32R)
        w_lo = sb("w_lo", [P, 3 * F], F32R)
        wo = sb("wo", [P, PAIRS, E])
        w1t_sb, w2_sb, w3_sb = sb("w1t_sb", [P, P]), sb("w2_sb", [P, P]), sb("w3_sb", [P, P])
        w12t_sb, wf = sb("w12t_sb", [P, P]), sb("wf", [P, P])
        bias_row, bias_all, ones_row = sb("bias_row", [1, P]), sb("bias_all", [P, TT, P]), sb("ones_row", [1, P])
        pe = sb("pe", [P, 2 * T])
        mask_raw, mask = sb("mask_raw", [P, 2 * P]), sb("mask", [P, 2 * P], BF16)
        ident, ident_b = sb("ident", [P, P]), sb("ident_b", [P, P], BF16)
        half_power = sb("half_power", [P, TT])

        def two(name, shape, dt=F32):
            return [sb(f"{name}{i}", shape, dt) for i in range(2)]

        x_in, x_res = two("x_in", [P, TT, E]), two("x_res", [P, TT, E])
        xn = two("xn", [P, TT, E])
        xt_hi, xt_lo = two("xt_hi", [P, T], F32R), two("xt_lo", [P, T], F32R)
        vals = two("vals", [P, TT, F])
        heads_t = two("heads_t", [P, PAIRS, T])
        attn_n, x1, yn = two("attn_n", [P, TT, E]), two("x1", [P, TT, E]), two("yn", [P, TT, E])
        yt = two("yt", [P, T])
        ffn_in, ffn_th, ffn_n, x2 = (two(n, [P, TT, E]) for n in ("ffn_in", "ffn_th", "ffn_n", "x2"))
        qk = two("qk", [P, 2 * T])
        neg_max, row_sum, inv_sum = two("neg_max", [P, 4]), two("row_sum", [P, 4]), two("inv_sum", [P, 4])
        probs = two("probs", [P, 2, SC])
        pt0, pt1 = two("pt0", [P, 2, T]), two("pt1", [P, 2, P])

        consts_in = sem("consts_in")
        x_loaded, res_loaded, stored = ([sem(f"{n}{i}") for i in range(2)] for n in ("x_loaded", "res_loaded", "stored"))
        ready_dve, ready_split, fused_pe, fused_dve = sem("ready_dve"), sem("ready_split"), sem("fused_pe"), sem("fused_dve")
        qk_made, qk_kept = sem("qk_made"), sem("qk_kept")
        scores_made, max_found, exps_done = sem("scores_made"), sem("max_found"), sem("exps_done")
        inv_found, probs_ready = sem("inv_found"), sem("probs_ready")
        turned0, turned1, pt0_kept, pt1_kept = sem("turned0"), sem("turned1"), sem("pt0_kept"), sem("pt1_kept")
        heads_made, heads_kept = sem("heads_made"), sem("heads_kept")
        vals_made, vals_kept = sem("vals_made"), sem("vals_kept")
        x_turned, x_hi_kept, x_lo_kept = sem("x_turned"), sem("x_hi_kept"), sem("x_lo_kept")
        attn_made, x1_made, out_made = sem("attn_made"), sem("x1_made"), sem("out_made")
        y_turned, y_kept, ffn_made, ffn_kept, tanh_done = (
            sem(n) for n in ("y_turned", "y_kept", "ffn_made", "ffn_kept", "tanh_done"))
        norms = {}
        for n in ("x", "attn", "y", "ffn"):
            norms[n] = dict(
                stats=sb(f"{n}_stats", [P, TT, 6]), moments=sb(f"{n}_moments", [P, TT, 2]),
                var_eps=sb(f"{n}_var_eps", [P, TT]), rstd=sb(f"{n}_rstd", [P, TT]),
                moments_taken=sem(f"{n}_moments_taken"),
                eps_added=sem(f"{n}_eps_added"), rstd_made=sem(f"{n}_rstd_made"), normed=sem(f"{n}_normed"))

        def pair(b, p):
            return b.times(PAIRS, p)

        def pair_exists(b, p):
            g = pair(b, p)
            return not isinstance(g, int) or 0 <= g < G

        def batch_of(b, p):
            q, p = divmod(p, PAIRS)
            return b.plus(q), p

        def all_slots(eng, slot):
            for b in range(-2, 4):
                for p in range(3 if b == -2 else 0, PAIRS):
                    slot(Batch(b // 2, b % 2, B), p)
            with eng.Fori(2, B // 2 - 1) as half:
                for parity in range(2):
                    for p in range(PAIRS):
                        slot(Batch(half, parity, B), p)
            for b in range(B - 2, B + 2):
                for p in range(3 if b == B + 1 else PAIRS):
                    slot(Batch(b // 2, b % 2, B), p)

        block = ctx.enter_context(nc.Block())

        @block.sync
        def _(sp):
            def load(b, dst, loaded):
                sp.dma_start(dst[b.parity][:, :, :], rows(x_dram, b)).then_inc(loaded[b.parity], 16)

            def rows(dram, b):
                n = b.times(1)
                view = dram[:, n, :, :] if isinstance(n, int) else dram[:, bass.ds(n, 1), :, :]
                return view if isinstance(n, int) else view.rearrange("p a t e -> p (a t) e")

            def slot(b, p):
                if p == 0 and b.plus(3).exists():
                    wait(sp, norms["x"]["normed"], b.times(1, 2))
                    load(b.plus(3), x_in, x_loaded)
                if p == 2 and b.plus(1).exists():
                    wait(sp, x1_made, b.times(1))
                    load(b.plus(1), x_res, res_loaded)
                if p == 3 and b.plus(-2).exists():
                    c = b.plus(-2)
                    sp.wait_ge(out_made, c.times(1, 1))
                    sp.dma_start(rows(out_dram, c), x2[c.parity][:, :, :]).then_inc(stored[c.parity], 16)

            load(Batch(0, 0, B), x_in, x_loaded)
            load(Batch(0, 1, B), x_in, x_loaded)
            for b in range(-1, 4):
                for p in range(PAIRS):
                    slot(Batch(b // 2, b % 2, B), p)
            with sp.Fori(2, B // 2 - 2) as half:
                for parity in range(2):
                    for p in range(PAIRS):
                        slot(Batch(half, parity, B), p)
            for b in range(B - 4, B + 2):
                for p in range(PAIRS):
                    slot(Batch(b // 2, b % 2, B), p)
            sp.wait_ge(stored[0], 16 * (B // 2))
            sp.wait_ge(stored[1], 16 * (B // 2))

        @block.scalar
        def _(act):
            act.dma_start(ident[:, :], ident_dram).then_inc(consts_in, 16)
            act.dma_start(w_raw[:, :], w_qkv_t).then_inc(consts_in, 16)
            act.dma_start(pe[:, :], pe_dram).then_inc(consts_in, 16)
            act.dma_start(mask_raw[:, :], mask_dram).then_inc(consts_in, 16)
            act.dma_start(wo[:, :, :], w_o_t.rearrange("(c f) e -> f c e", f=P)).then_inc(consts_in, 16)
            act.dma_start(w1t_sb[:, :], w1_t).then_inc(consts_in, 16)
            act.dma_start(w2_sb[:, :], w2).then_inc(consts_in, 16)
            act.dma_start(w3_sb[:, :], w3).then_inc(consts_in, 16)
            act.dma_start(bias_row[:, :], bias.rearrange("(a n) -> a n", a=1)).then_inc(consts_in, 16)

            def exps(b, p):
                g = pair(b, p)
                i = p % 2
                wait(act, turned0, pair(b, p - 1))
                for h in range(2):
                    act.wait_ge(max_found, b.times(2 * PAIRS, 2 * p + h + 1))
                    for j, (lo, hi) in enumerate(((T, SC), (0, T))):
                        k = 2 * h + j
                        ins = nc.scalar.activation(probs[i][:, h, lo:hi], s_bank[h][i][:, lo:hi], ACT.Exp,
                                                   bias=neg_max[i][:, k:k + 1], accum_out=row_sum[i][:, k:k + 1])
                    ins.then_inc(exps_done, 1)

            def keep_vals(b, t):
                act.wait_ge(vals_made, b.times(2, t + 1))
                wait(act, heads_made, pair(b, -PAIRS))
                nc.scalar.copy(vals[b.parity][:, t, :], misc_bank[:, :]).then_inc(vals_kept, 1)

            def keep_turned(b, p):
                i = p % 2
                if pair_exists(b, p):
                    act.wait_ge(turned1, pair(b, p + 1))
                    wait(act, heads_made, pair(b, p - 1))
                    nc.scalar.copy(pt1[i][:, :, :], turn_out_bank[:, 0:2 * P].rearrange("p (h t) -> p h t", h=2)
                                   ).then_inc(pt1_kept, 1)
                if pair_exists(b, p - 1):
                    c, q = batch_of(b, p - 1)
                    act.wait_ge(heads_made, pair(b, p))
                    wait(act, attn_made, c.times(1, -1))
                    nc.scalar.copy(heads_t[c.parity][:, q, :], turn_out_bank[:, T:2 * T]).then_inc(heads_kept, 1)
                if pair_exists(b, p):
                    act.wait_ge(turned0, pair(b, p + 1))
                    nc.scalar.copy(pt0[i][:, :, :], turn_bank[:, :, :]).then_inc(pt0_kept, 1)

            def slot(b, p):
                if p == 0 and b.exists():
                    keep_vals(b, 1)
                if p == 3 and b.plus(1).exists():
                    keep_vals(b.plus(1), 0)
                if p == 1 and b.plus(-2).exists():
                    c = b.plus(-2)
                    act.wait_ge(ffn_kept, c.times(1, 1))
                    wait(act, norms["ffn"]["normed"], c.times(1, -1))
                    nc.scalar.activation(ffn_th[c.parity][:, :, :], ffn_in[c.parity][:, :, :], ACT.Tanh
                                         ).then_inc(tanh_done, 1)
                if pair_exists(b, p + 1):
                    exps(*batch_of(b, p + 1))
                if p == 0 and b.plus(1).exists():
                    c = b.plus(1)
                    act.wait_ge(x_turned, c.times(1, 1))
                    wait(act, qk_made, pair(c, -PAIRS))
                    wait(act, vals_made, c.times(2, -2))
                    nc.scalar.copy(xt_hi[c.parity][:, :], misc_bank[:, 0:T]).then_inc(x_hi_kept, 1)
                if p == 3 and b.plus(-1).exists():
                    c = b.plus(-1)
                    act.wait_ge(y_turned, c.times(1, 1))
                    wait(act, ffn_made, c.times(1, -1))
                    nc.scalar.copy(yt[c.parity][:, :], misc_bank[:, 0:T]).then_inc(y_kept, 1)
                keep_turned(b, p)

            all_slots(act, slot)

        @block.gpsimd
        def _(pool):
            nc.gpsimd.memset(half_power[:, :], -0.5).then_inc(ready_dve, 1)
            pool.wait_ge(ready_dve, 1)

            def rstd(name, b):
                n = norms[name]
                pool.wait_ge(n["eps_added"], b.times(1, 1))
                wait(pool, n["normed"], b.times(1))
                nc.gpsimd.tensor_tensor(n["rstd"][:, :], n["var_eps"][:, :], half_power[:, :], ALU.pow
                                        ).then_inc(n["rstd_made"], 1)

            def slot(b, p):
                if p == 3 and b.plus(2).exists():
                    rstd("x", b.plus(2))
                if p == 1 and b.plus(-2).exists():
                    rstd("ffn", b.plus(-2))
                if p == 1 and b.plus(-1).exists():
                    rstd("attn", b.plus(-1))
                if p == 2 and b.plus(-1).exists():
                    c = b.plus(-1)
                    pool.wait_ge(norms["attn"]["normed"], c.times(1, 1))
                    pool.wait_ge(res_loaded[c.parity], (c.half + 1) * 16)
                    wait(pool, out_made, c.times(1, -1))
                    wait(pool, norms["y"]["normed"], c.times(1, -1))
                    nc.gpsimd.tensor_tensor(x1[c.parity][:, :, :], attn_n[c.parity][:, :, :],
                                            x_res[c.parity][:, :, :], ALU.add).then_inc(x1_made, 1)
                if p == 2 and b.plus(-2).exists():
                    c = b.plus(-2)
                    pool.wait_ge(norms["ffn"]["normed"], c.times(1, 1))
                    pool.wait_ge(x1_made, c.times(1, 1))
                    wait(pool, stored[c.parity], c.half * 16)
                    nc.gpsimd.tensor_tensor(x2[c.parity][:, :, :], ffn_n[c.parity][:, :, :],
                                            x1[c.parity][:, :, :], ALU.add).then_inc(out_made, 1)
                if p == 2 and b.plus(-1).exists():
                    rstd("y", b.plus(-1))

            all_slots(pool, slot)

        @block.vector
        def _(dve):
            dve.wait_ge(consts_in, 16 * 9)
            nc.vector.memset(ones_row[:, :], 1.0)
            nc.vector.tensor_copy(ident_b[:, :], ident[:, :])
            nc.vector.tensor_copy(mask[:, :], mask_raw[:, :]).then_inc(ready_dve, 1)
            nc.vector.tensor_scalar(w_raw[:, 0:F], w_raw[:, 0:F], SCALE, None, ALU.mult).then_inc(ready_split, 1)
            dve.wait_ge(ready_split, 1)
            nc.vector.tensor_copy(w_hi[:, :], w_raw[:, :]).then_inc(ready_split, 1)
            dve.wait_ge(ready_split, 2)
            nc.vector.tensor_tensor(w_lo[:, :], w_raw[:, :], w_hi[:, :].bitcast(F32), ALU.subtract
                                    ).then_inc(ready_split, 1)
            dve.wait_ge(fused_pe, 1)
            nc.vector.tensor_copy(w12t_sb[:, :], misc_bank[:, 0:P]).then_inc(fused_dve, 1)
            dve.wait_ge(fused_pe, 2)
            nc.vector.tensor_copy(wf[:, :], misc_bank[:, P:2 * P])
            nc.vector.tensor_copy(bias_all[:, 0, :], misc_bank[:, 2 * P:3 * P])
            nc.vector.tensor_copy(bias_all[:, 1, :], misc_bank[:, 2 * P:3 * P]).then_inc(fused_dve, 1)

            def take_moments(name, b, source):
                n = norms[name]
                for t in range(TT):
                    ins = nc.vector.bn_stats(n["stats"][:, t, :], source(t))
                nc.vector.drain()
                for t in range(TT):
                    ins = nc.vector.bn_aggr(n["moments"][:, t, :], n["stats"][:, t, :])
                ins.then_inc(n["moments_taken"], 1)
                dve.wait_ge(n["moments_taken"], b.times(1, 1))
                wait(dve, n["rstd_made"], b.times(1))
                nc.vector.tensor_scalar(n["var_eps"][:, :], n["moments"][:, :, 1], EPS, None, ALU.add
                                        ).then_inc(n["eps_added"], 1)

            def normalise(name, b, source, to):
                n = norms[name]
                dve.wait_ge(n["rstd_made"], b.times(1, 1))
                for t in range(TT):
                    ins = nc.vector.tensor_scalar(to[:, t, :], source(t), n["moments"][:, t, 0:1],
                                                  n["rstd"][:, t:t + 1], ALU.subtract, ALU.mult)
                ins.then_inc(n["normed"], 1)

            def attn_rows(t):
                return misc_bank[:, t * E:(t + 1) * E]

            def row_max(b, p):
                i = p % 2
                wait(dve, exps_done, b.times(2 * PAIRS, 2 * p - 2))
                for h in range(2):
                    dve.wait_ge(scores_made, b.times(2 * PAIRS, 2 * p + h + 1))
                    for j, (lo, hi) in enumerate(((T, SC), (0, T))):
                        k = 2 * h + j
                        ins = nc.vector.tensor_reduce(neg_max[i][:, k:k + 1], s_bank[h][i][:, lo:hi], AX_X, ALU.max,
                                                      negate=True)
                    ins.then_inc(max_found, 1)

            def keep_qk(b, p):
                dve.wait_ge(qk_made, pair(b, p + 1))
                wait(dve, scores_made, b.times(2 * PAIRS, 2 * p - 2))
                nc.vector.tensor_tensor(qk[p % 2][:, :], qk_bank[:, :], pe[:, :], ALU.add).then_inc(qk_kept, 1)

            def scale_probs(b, p):
                i = p % 2
                for h in range(2):
                    n = b.times(2 * PAIRS, 2 * p + h + 1)
                    dve.wait_ge(exps_done, n)
                    nc.vector.reciprocal(inv_sum[i][:, 2 * h:2 * h + 2], row_sum[i][:, 2 * h:2 * h + 2]
                                         ).then_inc(inv_found, 1)
                    dve.wait_ge(inv_found, n)
                    for j, (lo, hi) in enumerate(((T, SC), (0, T))):
                        k = 2 * h + j
                        ins = nc.vector.tensor_scalar(probs[i][:, h, lo:hi], probs[i][:, h, lo:hi],
                                                      inv_sum[i][:, k:k + 1], None, ALU.mult)
                    ins.then_inc(probs_ready, 1)

            def slot(b, p):
                if pair_exists(b, p + 1):
                    row_max(*batch_of(b, p + 1))
                if p == 0 and b.plus(1).exists():
                    c = b.plus(1)
                    wait(dve, x_turned, c.times(1, -1))
                    normalise("x", c, lambda t: x_in[c.parity][:, t, :], xn[c.parity])
                if p == 2 and b.plus(-1).exists():
                    c = b.plus(-1)
                    wait(dve, x1_made, c.times(1, -1))
                    normalise("attn", c, attn_rows, attn_n[c.parity])
                if p == 2 and b.plus(-2).exists():
                    c = b.plus(-2)
                    wait(dve, out_made, c.times(1, -1))
                    normalise("ffn", c, lambda t: ffn_th[c.parity][:, t, :], ffn_n[c.parity])
                if p == 3 and b.plus(-1).exists():
                    c = b.plus(-1)
                    wait(dve, y_turned, c.times(1, -1))
                    normalise("y", c, lambda t: x1[c.parity][:, t, :], yn[c.parity])
                if pair_exists(b, p + 2):
                    keep_qk(*batch_of(b, p + 2))
                if p == 0 and b.plus(1).exists():
                    c = b.plus(1)
                    dve.wait_ge(x_hi_kept, c.times(1, 1))
                    wait(dve, qk_made, pair(c, -PAIRS))
                    wait(dve, vals_made, c.times(2, -2))
                    nc.vector.tensor_tensor(xt_lo[c.parity][:, :], misc_bank[:, 0:T], xt_hi[c.parity][:, :].bitcast(F32),
                                            ALU.subtract).then_inc(x_lo_kept, 1)
                if p == 0 and b.plus(-2).exists():
                    c = b.plus(-2)
                    dve.wait_ge(ffn_made, c.times(1, 1))
                    wait(dve, tanh_done, c.times(1, -1))
                    nc.vector.tensor_tensor(ffn_in[c.parity][:, :, :],
                                            misc_bank[:, T:2 * T].rearrange("p (t e) -> p t e", t=TT),
                                            bias_all[:, :, :], ALU.add).then_inc(ffn_kept, 1)
                if pair_exists(b, p + 1):
                    scale_probs(*batch_of(b, p + 1))
                if p == 1 and b.plus(-2).exists():
                    c = b.plus(-2)
                    dve.wait_ge(tanh_done, c.times(1, 1))
                    take_moments("ffn", c, lambda t: ffn_th[c.parity][:, t, :])
                if p == 1 and b.plus(-1).exists():
                    c = b.plus(-1)
                    dve.wait_ge(attn_made, c.times(1, 1))
                    take_moments("attn", c, attn_rows)
                if p == 2 and b.plus(-1).exists():
                    c = b.plus(-1)
                    dve.wait_ge(x1_made, c.times(1, 1))
                    take_moments("y", c, lambda t: x1[c.parity][:, t, :])
                if p == 3 and b.plus(2).exists():
                    c = b.plus(2)
                    dve.wait_ge(x_loaded[c.parity], (c.half + 1) * 16)
                    take_moments("x", c, lambda t: x_in[c.parity][:, t, :])

            all_slots(dve, slot)

        @block.tensor
        def _(pe_eng):
            mm = nc.tensor.matmul
            pe_eng.wait_ge(ready_dve, 2)
            mm(misc_bank[:, 0:P], w2_sb[:, :], w1t_sb[:, :], start=True, stop=True).then_inc(fused_pe, 1)
            pe_eng.wait_ge(fused_dve, 1)
            mm(misc_bank[:, P:2 * P], w12t_sb[:, :], w3_sb[:, :], start=True, stop=True)
            mm(misc_bank[:, 2 * P:3 * P], ones_row[:, :], bias_row[:, :], start=True, stop=True).then_inc(fused_pe, 1)
            pe_eng.wait_ge(ready_split, 3)
            pe_eng.wait_ge(fused_dve, 2)

            def make_vals(b, t):
                hi, lo = xt_hi[b.parity][:, t * P:(t + 1) * P], xt_lo[b.parity][:, t * P:(t + 1) * P]
                v = slice(2 * F, 3 * F)
                mm(misc_bank[:, :], hi, w_hi[:, v], start=True, stop=False)
                mm(misc_bank[:, :], hi, w_lo[:, v], start=False, stop=False)
                mm(misc_bank[:, :], lo, w_hi[:, v], start=False, stop=True).then_inc(vals_made, 1)

            def make_scores(b, p):
                i = p % 2
                pe_eng.wait_ge(qk_kept, pair(b, p + 1))
                wait(pe_eng, exps_done, b.times(2 * PAIRS, 2 * p - 2))
                for q_lo, k_hi, at in ((P, T, 0), (0, P, T)):
                    for h in range(2):
                        r = slice(h * D, (h + 1) * D)
                        mm(s_bank[h][i][:, at:at + k_hi], qk[i][r, q_lo:q_lo + P], qk[i][r, T:T + k_hi],
                           start=(at == 0), stop=False)
                for h in range(2):
                    mm(s_bank[h][i][:, P:SC], ident_b[:, :], mask[:, :], start=False, stop=True
                       ).then_inc(scores_made, 1)

            def make_qk(b, p):
                pe_eng.wait_ge(x_lo_kept, b.times(1, 1))
                wait(pe_eng, qk_kept, pair(b, p))
                hi, lo = xt_hi[b.parity], xt_lo[b.parity]
                for part in range(2):
                    f = slice(part * F + p * P, part * F + (p + 1) * P)
                    to = qk_bank[:, part * T:(part + 1) * T]
                    mm(to, w_hi[:, f], hi[:, :], start=True, stop=False)
                    mm(to, w_hi[:, f], lo[:, :], start=False, stop=False)
                    ins = mm(to, w_lo[:, f], hi[:, :], start=False, stop=True)
                ins.then_inc(qk_made, 1)

            def make_heads(b, p):
                i = p % 2
                pe_eng.wait_ge(pt0_kept, pair(b, p + 1))
                pe_eng.wait_ge(vals_kept, b.times(2, 2))
                wait(pe_eng, heads_kept, pair(b, p))
                for s, to, rhs in ((0, slice(T, 2 * T), pt0), (1, slice(T + P, 2 * T), pt1)):
                    for h in range(2):
                        f = (2 * p + h) * D
                        ins = mm(turn_out_bank[h * D:(h + 1) * D, to], vals[b.parity][:, s, f:f + D], rhs[i][:, h, :],
                                 start=(s == 0), stop=(s == 1))
                ins.then_inc(heads_made, 1)

            def turn_probs(b, p):
                i = p % 2
                pe_eng.wait_ge(probs_ready, b.times(2 * PAIRS, 2 * p + 2))
                wait(pe_eng, pt0_kept, pair(b, p))
                for h in range(2):
                    ins = nc.tensor.transpose(turn_out_bank[:, h * P:(h + 1) * P], probs[i][:, h, P:T], ident[:, :])
                ins.then_inc(turned1, 1)
                for h in range(2):
                    nc.tensor.transpose(turn_bank[:, h, P:T], probs[i][:, h, 0:P], ident[:, :])
                    ins = nc.tensor.transpose(turn_bank[:, h, 0:P], probs[i][:, h, T:SC], ident[:, :])
                ins.then_inc(turned0, 1)

            def turn_rows(source, made):
                for t in range(TT):
                    ins = nc.tensor.transpose(misc_bank[:, t * P:(t + 1) * P], source[:, t, :], ident[:, :])
                ins.then_inc(made, 1)

            def slot(b, p):
                if p == 0 and b.exists():
                    wait(pe_eng, y_kept, b.times(1, -1))
                    pe_eng.wait_ge(vals_kept, b.times(2, 1))
                    make_vals(b, 1)
                if p == 3 and b.plus(1).exists():
                    c = b.plus(1)
                    pe_eng.wait_ge(x_lo_kept, c.times(1, 1))
                    wait(pe_eng, norms["attn"]["normed"], b.times(1))
                    make_vals(c, 0)
                if pair_exists(b, p + 1):
                    make_scores(*batch_of(b, p + 1))
                if pair_exists(b, p + 2):
                    make_qk(*batch_of(b, p + 2))
                if p == 0 and b.plus(-2).exists():
                    c = b.plus(-2)
                    pe_eng.wait_ge(y_kept, c.times(1, 1))
                    if b.exists():
                        pe_eng.wait_ge(vals_kept, b.times(2, 2))
                    for t in range(TT):
                        ins = mm(misc_bank[:, T + t * E:T + (t + 1) * E], yt[c.parity][:, t * P:(t + 1) * P], wf[:, :],
                                 start=True, stop=True)
                    ins.then_inc(ffn_made, 1)
                if p == 0 and b.plus(1).exists():
                    c = b.plus(1)
                    pe_eng.wait_ge(norms["x"]["normed"], c.times(1, 1))
                    if b.exists():
                        pe_eng.wait_ge(vals_kept, b.times(2, 2))
                    turn_rows(xn[c.parity], x_turned)
                if p == 1 and b.plus(-1).exists():
                    c = b.plus(-1)
                    pe_eng.wait_ge(heads_kept, pair(b, 0))
                    if b.plus(1).exists():
                        pe_eng.wait_ge(x_lo_kept, b.times(1, 2))
                    wait(pe_eng, ffn_kept, b.times(1, -1))
                    for t in range(TT):
                        for k in range(PAIRS):
                            ins = mm(misc_bank[:, t * E:(t + 1) * E], heads_t[c.parity][:, k, t * P:(t + 1) * P],
                                     wo[:, k, :], start=(k == 0), stop=(k == PAIRS - 1))
                    ins.then_inc(attn_made, 1)
                if p == 3 and b.plus(-1).exists():
                    c = b.plus(-1)
                    pe_eng.wait_ge(norms["y"]["normed"], c.times(1, 1))
                    if b.plus(1).exists():
                        pe_eng.wait_ge(vals_kept, b.times(2, 3))
                    turn_rows(yn[c.parity], y_turned)
                if pair_exists(b, p - 1):
                    make_heads(*batch_of(b, p - 1))
                if pair_exists(b, p):
                    turn_probs(b, p)

            all_slots(pe_eng, slot)


def kernel(L0_attn_x, L0_attn_Wqkv, L0_attn_Wo, L0_ffn_weight, L0_ffn_aux_weight1, L0_ffn_aux_weight2, L0_ffn_bias):
    import numpy as _np
    import concourse.bacc as _bacc
    from concourse import mybir as _mybir
    from concourse.bass_utils import run_bass_kernel_spmd as _run

    B, T, E = L0_attn_x.shape
    H = 8
    D = L0_attn_Wo.shape[1] // H
    w_qkv_t = _np.asarray(L0_attn_Wqkv).reshape(H, 3, D, E).transpose(3, 1, 0, 2).reshape(E, 3 * H * D)
    inputs = {
        "x": L0_attn_x,
        "w_qkv_t": w_qkv_t,
        "w_o_t": _np.asarray(L0_attn_Wo).T,
        "w1_t": _np.asarray(L0_ffn_weight).T,
        "w2": L0_ffn_aux_weight1,
        "w3": L0_ffn_aux_weight2,
        "bias": L0_ffn_bias,
    }
    nc = _bacc.Bacc("TRN2", target_bir_lowering=False, num_devices=1)
    arrays, args = {}, []
    for name, a in inputs.items():
        a = _np.ascontiguousarray(a)
        arrays[f"in_{name}"] = a
        args.append(nc.dram_tensor(f"in_{name}", a.shape, _mybir.dt.from_np(a.dtype), kind="ExternalInput").ap())
    out = nc.dram_tensor("out_x", (B, T, E), _mybir.dt.from_np(_np.dtype("float32")), kind="ExternalOutput").ap()
    build_block(nc, *args, out, H)
    r = _run(nc, [arrays], core_ids=[0])
    return r.results[0]["out_x"]
```

```python
from contextlib import ExitStack

import numpy as np

import concourse.bass as bass
from concourse import mybir

ALU = mybir.AluOpType
ACT = mybir.ActivationFunctionType
AX_X = mybir.AxisListType.X
F32 = mybir.dt.float32
F32R = mybir.dt.float32r
BF16 = mybir.dt.bfloat16

P = 128
EPS = 1e-5
MASKED = -3.0e38


class Batch:

    def __init__(self, half, parity, total):
        self.half, self.parity, self.total = half, parity, total

    def plus(self, n):
        q, parity = divmod(self.parity + n, 2)
        return Batch(self.half + q, parity, self.total)

    def times(self, k, add=0):
        return self.half * (2 * k) + (k * self.parity + add)

    def exists(self):
        return not isinstance(self.half, int) or 0 <= 2 * self.half + self.parity < self.total


def wait(eng, sem, value):
    if not isinstance(value, int) or value > 0:
        eng.wait_ge(sem, value)


def constants(T, D):
    pos = np.arange(T, dtype=np.float32)[:, None]
    div = np.exp(np.arange(0, D, 2, dtype=np.float32) * np.float32(-np.log(10000.0) / D))
    ang = (pos * div.astype(np.float32)).astype(np.float32)
    pe = np.stack([np.sin(ang), np.cos(ang)], axis=-1).reshape(T, D).astype(np.float32)
    pe_t = np.concatenate([pe.T, pe.T], axis=0)
    scale = np.float32(D ** -0.5)
    pe_qk = np.concatenate([pe_t * scale, pe_t], axis=1)
    causal = np.where(np.arange(P)[None, :] <= np.arange(P)[:, None], 0.0, MASKED).astype(np.float32)
    mask = np.concatenate([causal, causal], axis=1)
    return np.ascontiguousarray(pe_qk), np.ascontiguousarray(mask), np.eye(P, dtype=np.float32)


def build_block(nc, x, w_qkv_t, w_o_t, w1_t, w2, w3, bias, out, H):
    B, T, E = x.shape
    D = w_o_t.shape[0] // H
    TT = T // P
    PAIRS = H // 2
    F = H * D
    SCALE = float(D) ** -0.5
    assert E == P and TT == 2 and 2 * D == P and PAIRS == 4 and B % 2 == 0 and B >= 10
    G = B * PAIRS
    SC = T + P

    pe_np, mask_np, ident_np = constants(T, D)
    pe_dram = nc.inline_tensor(pe_np, name="pe_table").ap()
    mask_dram = nc.inline_tensor(mask_np, name="causal_mask").ap()
    ident_dram = nc.inline_tensor(ident_np, name="identity").ap()

    x_dram = x.rearrange("b (t p) e -> p b t e", p=P)
    out_dram = out.rearrange("b (t p) e -> p b t e", p=P)

    with ExitStack() as ctx:
        def sb(name, shape, dt=F32):
            return ctx.enter_context(nc.sbuf_tensor(name, shape, dt))

        def sem(name):
            return ctx.enter_context(nc.semaphore(name))

        s_bank = [[ctx.enter_context(nc.psum_tensor(f"scores_{h}_{i}", [P, 512], F32)) for i in range(2)]
                  for h in range(2)]
        turn_bank = ctx.enter_context(nc.psum_tensor("turned_probs", [P, 2, T], F32))
        turn_out_bank = ctx.enter_context(nc.psum_tensor("turned_probs_and_heads", [P, 512], F32))
        qk_bank = ctx.enter_context(nc.psum_tensor("qk_bank", [P, 512], F32))
        misc_bank = ctx.enter_context(nc.psum_tensor("misc_bank", [P, 512], F32))

        w_raw = sb("w_raw", [P, 3 * F])
        w_hi = sb("w_hi", [P, 3 * F], F32R)
        w_lo = sb("w_lo", [P, 3 * F], F32R)
        wo = sb("wo", [P, PAIRS, E])
        w1t_sb, w2_sb, w3_sb = sb("w1t_sb", [P, P]), sb("w2_sb", [P, P]), sb("w3_sb", [P, P])
        w12t_sb, wf = sb("w12t_sb", [P, P]), sb("wf", [P, P])
        bias_row, bias_all, ones_row = sb("bias_row", [1, P]), sb("bias_all", [P, TT, P]), sb("ones_row", [1, P])
        pe = sb("pe", [P, 2 * T])
        mask_raw, mask = sb("mask_raw", [P, 2 * P]), sb("mask", [P, 2 * P], BF16)
        ident, ident_b = sb("ident", [P, P]), sb("ident_b", [P, P], BF16)
        half_power = sb("half_power", [P, TT])

        def two(name, shape, dt=F32):
            return [sb(f"{name}{i}", shape, dt) for i in range(2)]

        x_in, x_res = two("x_in", [P, TT, E]), two("x_res", [P, TT, E])
        xn = two("xn", [P, TT, E])
        xt_hi, xt_lo = two("xt_hi", [P, T], F32R), two("xt_lo", [P, T], F32R)
        vals = two("vals", [P, TT, F])
        heads_t = two("heads_t", [P, PAIRS, T])
        attn_n, x1, yn = two("attn_n", [P, TT, E]), two("x1", [P, TT, E]), two("yn", [P, TT, E])
        yt = two("yt", [P, T])
        ffn_in, ffn_th, ffn_n, x2 = (two(n, [P, TT, E]) for n in ("ffn_in", "ffn_th", "ffn_n", "x2"))
        qk = two("qk", [P, 2 * T])
        neg_max, row_sum, inv_sum = two("neg_max", [P, 4]), two("row_sum", [P, 4]), two("inv_sum", [P, 2 * TT])
        probs = two("probs", [P, 2, SC])
        pt0, pt1 = two("pt0", [P, 2, T]), two("pt1", [P, 2, P])
        inv_wide, inv_all = two("inv_wide", [P, TT, 2, D]), two("inv_all", [P, T])

        consts_in = sem("consts_in")
        x_loaded, res_loaded, stored = ([sem(f"{n}{i}") for i in range(2)] for n in ("x_loaded", "res_loaded", "stored"))
        power_set = sem("power_set")
        ready_dve, ready_split, fused_pe, fused_dve = sem("ready_dve"), sem("ready_split"), sem("fused_pe"), sem("fused_dve")
        qk_made, qk_kept = sem("qk_made"), sem("qk_kept")
        scores_made, max_found, exps_done = sem("scores_made"), sem("max_found"), sem("exps_done")
        inv_found, inv_spread, inv_turned, inv_kept = sem("inv_found"), sem("inv_spread"), sem("inv_turned"), sem("inv_kept")
        turned0, turned1, pt0_kept, pt1_kept = sem("turned0"), sem("turned1"), sem("pt0_kept"), sem("pt1_kept")
        heads_made, heads_kept = sem("heads_made"), sem("heads_kept")
        vals_made, vals_kept = sem("vals_made"), sem("vals_kept")
        x_turned, x_hi_kept, x_lo_kept = sem("x_turned"), sem("x_hi_kept"), sem("x_lo_kept")
        attn_made, x1_made, out_made = sem("attn_made"), sem("x1_made"), sem("out_made")
        y_turned, y_kept, ffn_made, ffn_kept, tanh_done = (
            sem(n) for n in ("y_turned", "y_kept", "ffn_made", "ffn_kept", "tanh_done"))
        norms = {}
        for n in ("x", "attn", "y", "ffn"):
            norms[n] = dict(
                stats=sb(f"{n}_stats", [P, TT, 6]), moments=sb(f"{n}_moments", [P, TT, 2]),
                var_eps=sb(f"{n}_var_eps", [P, TT]), rstd=sb(f"{n}_rstd", [P, TT]),
                centered=sem(f"{n}_centered"), moments_taken=sem(f"{n}_moments_taken"),
                eps_added=sem(f"{n}_eps_added"), rstd_made=sem(f"{n}_rstd_made"), normed=sem(f"{n}_normed"))

        def pair(b, p):
            return b.times(PAIRS, p)

        def pair_exists(b, p):
            g = pair(b, p)
            return not isinstance(g, int) or 0 <= g < G

        def batch_of(b, p):
            q, p = divmod(p, PAIRS)
            return b.plus(q), p

        def all_slots(eng, slot, prepare=None):
            for b in range(-2, 4):
                if b == -1 and prepare is not None:
                    prepare()
                for p in range(1 if b == -2 else 0, PAIRS):
                    slot(Batch(b // 2, b % 2, B), p)
            with eng.Fori(2, B // 2 - 1) as half:
                for parity in range(2):
                    for p in range(PAIRS):
                        slot(Batch(half, parity, B), p)
            for b in range(B - 2, B + 2):
                for p in range(PAIRS):
                    slot(Batch(b // 2, b % 2, B), p)

        block = ctx.enter_context(nc.Block())

        @block.sync
        def _(sp):
            def load(b, dst, loaded):
                sp.dma_start(dst[b.parity][:, :, :], rows(x_dram, b)).then_inc(loaded[b.parity], 16)

            def rows(dram, b):
                n = b.times(1)
                view = dram[:, n, :, :] if isinstance(n, int) else dram[:, bass.ds(n, 1), :, :]
                return view if isinstance(n, int) else view.rearrange("p a t e -> p (a t) e")

            def slot(b, p):
                if p == 0 and b.plus(3).exists():
                    wait(sp, norms["x"]["normed"], b.times(1, 2))
                    load(b.plus(3), x_in, x_loaded)
                if p == 2 and b.plus(1).exists():
                    wait(sp, x1_made, b.times(1))
                    load(b.plus(1), x_res, res_loaded)
                if p == 3 and b.plus(-2).exists():
                    c = b.plus(-2)
                    sp.wait_ge(out_made, c.times(1, 1))
                    sp.dma_start(rows(out_dram, c), x2[c.parity][:, :, :]).then_inc(stored[c.parity], 16)

            load(Batch(0, 0, B), x_in, x_loaded)
            sp.dma_start(ident[:, :], ident_dram).then_inc(consts_in, 16)
            sp.dma_start(w1t_sb[:, :], w1_t).then_inc(consts_in, 16)
            sp.dma_start(w2_sb[:, :], w2).then_inc(consts_in, 16)
            sp.dma_start(w3_sb[:, :], w3).then_inc(consts_in, 16)
            load(Batch(0, 1, B), x_in, x_loaded)
            for b in range(-1, 4):
                for p in range(PAIRS):
                    slot(Batch(b // 2, b % 2, B), p)
            with sp.Fori(2, B // 2 - 2) as half:
                for parity in range(2):
                    for p in range(PAIRS):
                        slot(Batch(half, parity, B), p)
            for b in range(B - 4, B + 2):
                for p in range(PAIRS):
                    slot(Batch(b // 2, b % 2, B), p)
            sp.wait_ge(stored[0], 16 * (B // 2))
            sp.wait_ge(stored[1], 16 * (B // 2))

        @block.scalar
        def _(act):
            act.dma_start(w_raw[:, :], w_qkv_t).then_inc(consts_in, 16)
            act.dma_start(pe[:, :], pe_dram).then_inc(consts_in, 16)
            act.dma_start(mask_raw[:, :], mask_dram).then_inc(consts_in, 16)
            act.dma_start(wo[:, :, :], w_o_t.rearrange("(c f) e -> f c e", f=P)).then_inc(consts_in, 16)
            act.dma_start(bias_row[:, :], bias.rearrange("(a n) -> a n", a=1)).then_inc(consts_in, 16)

            def exps(b, p):
                g = pair(b, p)
                i = p % 2
                wait(act, turned0, pair(b, p - 1))
                for h in range(2):
                    act.wait_ge(max_found, b.times(2 * PAIRS, 2 * p + h + 1))
                    for j, (lo, hi) in enumerate(((T, SC), (0, T))):
                        k = 2 * j + h
                        ins = nc.scalar.activation(probs[i][:, h, lo:hi], s_bank[h][i][:, lo:hi], ACT.Exp,
                                                   bias=neg_max[i][:, k:k + 1], accum_out=row_sum[i][:, k:k + 1])
                    ins.then_inc(exps_done, 1)

            def keep_vals(b, t):
                act.wait_ge(vals_made, b.times(2, t + 1))
                wait(act, heads_made, pair(b, -PAIRS))
                nc.scalar.copy(vals[b.parity][:, t, :], misc_bank[:, :]).then_inc(vals_kept, 1)

            def keep_turned(b, p):
                i = p % 2
                act.wait_ge(turned1, pair(b, p + 1))
                wait(act, heads_made, pair(b, p - 1))
                nc.scalar.copy(pt1[i][:, :, :], turn_out_bank[:, 0:2 * P].rearrange("p (h t) -> p h t", h=2)
                               ).then_inc(pt1_kept, 1)
                act.wait_ge(turned0, pair(b, p + 1))
                nc.scalar.copy(pt0[i][:, :, :], turn_bank[:, :, :]).then_inc(pt0_kept, 1)

            def keep_inv(b, p):
                i = p % 2
                act.wait_ge(inv_turned, pair(b, p + 1))
                wait(act, heads_kept, pair(b, p - 1))
                for j in range(TT):
                    ins = nc.scalar.copy(inv_all[i][:, j * P:(j + 1) * P], s_bank[j][i][:, SC:SC + P])
                ins.then_inc(inv_kept, 1)

            def slot(b, p):
                if p == 3 and b.plus(-2).exists():
                    c = b.plus(-2)
                    act.wait_ge(ffn_kept, c.times(1, 1))
                    wait(act, norms["ffn"]["normed"], c.times(1, -1))
                    nc.scalar.activation(ffn_th[c.parity][:, :, :], ffn_in[c.parity][:, :, :], ACT.Tanh
                                         ).then_inc(tanh_done, 1)
                if pair_exists(b, p):
                    keep_inv(b, p)
                if p == 0 and b.exists():
                    keep_vals(b, 1)
                if pair_exists(b, p + 1):
                    exps(*batch_of(b, p + 1))
                if p == 3 and b.plus(1).exists():
                    keep_vals(b.plus(1), 0)
                if pair_exists(b, p):
                    keep_turned(b, p)
                if p == 0 and b.plus(-2).exists():
                    c = b.plus(-2)
                    act.wait_ge(y_turned, c.times(1, 1))
                    if b.plus(1).exists():
                        act.wait_ge(x_turned, b.times(1, 2))
                    wait(act, ffn_made, c.times(1, -1))
                    nc.scalar.copy(yt[c.parity][:, :], misc_bank[:, T:2 * T]).then_inc(y_kept, 1)
                if p == 0 and b.plus(1).exists():
                    c = b.plus(1)
                    act.wait_ge(x_turned, c.times(1, 1))
                    wait(act, qk_made, pair(c, -PAIRS))
                    wait(act, vals_made, c.times(2, -2))
                    nc.scalar.copy(xt_hi[c.parity][:, :], misc_bank[:, 0:T]).then_inc(x_hi_kept, 1)

            all_slots(act, slot)

        @block.gpsimd
        def _(pool):
            nc.gpsimd.memset(half_power[:, :], -0.5).then_inc(power_set, 1)
            pool.wait_ge(power_set, 1)

            def rstd(name, b):
                n = norms[name]
                pool.wait_ge(n["eps_added"], b.times(1, 1))
                wait(pool, n["normed"], b.times(1))
                nc.gpsimd.tensor_tensor(n["rstd"][:, :], n["var_eps"][:, :], half_power[:, :], ALU.pow
                                        ).then_inc(n["rstd_made"], 1)

            def normalise(name, b, source, to):
                n = norms[name]
                mean = n["moments"][:, :, 0:1].to_broadcast([P, TT, E])
                pool.wait_ge(n["rstd_made"], b.times(1, 1))
                nc.gpsimd.tensor_tensor(to[:, :, :], source[:, :, :], mean, ALU.subtract).then_inc(n["centered"], 1)
                pool.wait_ge(n["centered"], b.times(1, 1))
                nc.gpsimd.tensor_tensor(to[:, :, :], to[:, :, :], n["rstd"][:, :].unsqueeze(2).to_broadcast([P, TT, E]),
                                        ALU.mult).then_inc(n["normed"], 1)

            def slot(b, p):
                if p == 1 and b.plus(2).exists():
                    c = b.plus(2)
                    rstd("x", c)
                    wait(pool, x_turned, c.times(1, -1))
                    normalise("x", c, x_in[c.parity], xn[c.parity])
                if p == 2 and b.plus(-1).exists():
                    c = b.plus(-1)
                    rstd("attn", c)
                    pool.wait_ge(norms["attn"]["normed"], c.times(1, 1))
                    pool.wait_ge(res_loaded[c.parity], (c.half + 1) * 16)
                    wait(pool, out_made, c.times(1, -1))
                    wait(pool, norms["y"]["normed"], c.times(1, -1))
                    nc.gpsimd.tensor_tensor(x1[c.parity][:, :, :], attn_n[c.parity][:, :, :],
                                            x_res[c.parity][:, :, :], ALU.add).then_inc(x1_made, 1)
                if p == 3 and b.plus(-1).exists():
                    c = b.plus(-1)
                    rstd("y", c)
                    wait(pool, y_turned, c.times(1, -1))
                    normalise("y", c, x1[c.parity], yn[c.parity])
                if p == 3 and b.plus(-2).exists():
                    c = b.plus(-2)
                    rstd("ffn", c)
                    wait(pool, out_made, c.times(1, -1))
                    normalise("ffn", c, ffn_th[c.parity], ffn_n[c.parity])
                    pool.wait_ge(norms["ffn"]["normed"], c.times(1, 1))
                    pool.wait_ge(x1_made, c.times(1, 1))
                    wait(pool, stored[c.parity], c.half * 16)
                    nc.gpsimd.tensor_tensor(x2[c.parity][:, :, :], ffn_n[c.parity][:, :, :],
                                            x1[c.parity][:, :, :], ALU.add).then_inc(out_made, 1)

            all_slots(pool, slot)

        @block.vector
        def _(dve):
            def prepare():
                dve.wait_ge(consts_in, 16 * 9)
                nc.vector.memset(ones_row[:, :], 1.0)
                nc.vector.tensor_copy(ident_b[:, :], ident[:, :])
                nc.vector.tensor_copy(mask[:, :], mask_raw[:, :]).then_inc(ready_dve, 1)
                nc.vector.tensor_scalar(w_raw[:, 0:F], w_raw[:, 0:F], SCALE, None, ALU.mult).then_inc(ready_split, 1)
                dve.wait_ge(ready_split, 1)
                nc.vector.tensor_copy(w_hi[:, :], w_raw[:, :]).then_inc(ready_split, 1)
                dve.wait_ge(ready_split, 2)
                nc.vector.tensor_tensor(w_lo[:, :], w_raw[:, :], w_hi[:, :].bitcast(F32), ALU.subtract
                                        ).then_inc(ready_split, 1)
                dve.wait_ge(fused_pe, 1)
                nc.vector.tensor_copy(w12t_sb[:, :], misc_bank[:, 0:P]).then_inc(fused_dve, 1)
                dve.wait_ge(fused_pe, 2)
                nc.vector.tensor_copy(wf[:, :], misc_bank[:, P:2 * P])
                nc.vector.tensor_copy(bias_all[:, 0, :], misc_bank[:, 2 * P:3 * P])
                nc.vector.tensor_copy(bias_all[:, 1, :], misc_bank[:, 2 * P:3 * P]).then_inc(fused_dve, 1)

            def take_moments(name, b, source):
                n = norms[name]
                wait(dve, n["normed"], b.times(1))
                for t in range(TT):
                    ins = nc.vector.bn_stats(n["stats"][:, t, :], source(t))
                nc.vector.drain()
                for t in range(TT):
                    ins = nc.vector.bn_aggr(n["moments"][:, t, :], n["stats"][:, t, :])
                ins.then_inc(n["moments_taken"], 1)
                dve.wait_ge(n["moments_taken"], b.times(1, 1))
                nc.vector.tensor_scalar(n["var_eps"][:, :], n["moments"][:, :, 1], EPS, None, ALU.add
                                        ).then_inc(n["eps_added"], 1)

            def normalise(name, b, source, to):
                n = norms[name]
                dve.wait_ge(n["rstd_made"], b.times(1, 1))
                for t in range(TT):
                    ins = nc.vector.tensor_scalar(to[:, t, :], source(t), n["moments"][:, t, 0:1],
                                                  n["rstd"][:, t:t + 1], ALU.subtract, ALU.mult)
                ins.then_inc(n["normed"], 1)

            def attn_rows(t):
                return misc_bank[:, t * E:(t + 1) * E]

            def row_max(b, p):
                i = p % 2
                wait(dve, exps_done, b.times(2 * PAIRS, 2 * p - 2))
                for h in range(2):
                    dve.wait_ge(scores_made, b.times(2 * PAIRS, 2 * p + h + 1))
                    for j, (lo, hi) in enumerate(((T, SC), (0, T))):
                        k = 2 * j + h
                        ins = nc.vector.tensor_reduce(neg_max[i][:, k:k + 1], s_bank[h][i][:, lo:hi], AX_X, ALU.max,
                                                      negate=True)
                    ins.then_inc(max_found, 1)

            def keep_qk(b, p):
                dve.wait_ge(qk_made, pair(b, p + 1))
                wait(dve, scores_made, b.times(2 * PAIRS, 2 * p - 2))
                nc.vector.tensor_tensor(qk[p % 2][:, :], qk_bank[:, :], pe[:, :], ALU.add).then_inc(qk_kept, 1)

            def invert_sums(b, p):
                i = p % 2
                dve.wait_ge(exps_done, b.times(2 * PAIRS, 2 * p + 2))
                nc.vector.reciprocal(inv_sum[i][:, :], row_sum[i][:, :]).then_inc(inv_found, 1)
                wait(dve, inv_turned, pair(b, p - 1))
                dve.wait_ge(inv_found, pair(b, p + 1))
                every = inv_sum[i][:, :].rearrange("p (t h) -> p t h", t=TT).unsqueeze(3).to_broadcast([P, TT, 2, D])
                nc.vector.tensor_copy(inv_wide[i][:, :, :, :], every).then_inc(inv_spread, 1)

            def keep_heads(b, p):
                dve.wait_ge(heads_made, pair(b, p + 1))
                dve.wait_ge(inv_kept, pair(b, p + 1))
                if pair_exists(b, p + 1):
                    dve.wait_ge(pt1_kept, pair(b, p + 2))
                wait(dve, attn_made, b.times(1, -1))
                nc.vector.tensor_tensor(heads_t[b.parity][:, p, :], turn_out_bank[:, T:2 * T], inv_all[p % 2][:, :],
                                        ALU.mult).then_inc(heads_kept, 1)

            def slot(b, p):
                if p == 1 and b.plus(1).exists():
                    c = b.plus(1)
                    dve.wait_ge(x_hi_kept, c.times(1, 1))
                    wait(dve, qk_made, pair(c, -PAIRS))
                    wait(dve, vals_made, c.times(2, -2))
                    nc.vector.tensor_tensor(xt_lo[c.parity][:, :], misc_bank[:, 0:T], xt_hi[c.parity][:, :].bitcast(F32),
                                            ALU.subtract).then_inc(x_lo_kept, 1)
                if pair_exists(b, p + 1):
                    row_max(*batch_of(b, p + 1))
                if pair_exists(b, p + 2):
                    keep_qk(*batch_of(b, p + 2))
                if p == 1 and b.plus(2).exists():
                    c = b.plus(2)
                    dve.wait_ge(x_loaded[c.parity], (c.half + 1) * 16)
                    take_moments("x", c, lambda t: x_in[c.parity][:, t, :])
                if p == 2 and b.plus(-2).exists():
                    c = b.plus(-2)
                    dve.wait_ge(ffn_made, c.times(1, 1))
                    if b.plus(-1).exists():
                        dve.wait_ge(attn_made, b.times(1))
                    wait(dve, tanh_done, c.times(1, -1))
                    nc.vector.tensor_tensor(ffn_in[c.parity][:, :, :],
                                            misc_bank[:, T:2 * T].rearrange("p (t e) -> p t e", t=TT),
                                            bias_all[:, :, :], ALU.add).then_inc(ffn_kept, 1)
                if p == 2 and b.plus(-1).exists():
                    c = b.plus(-1)
                    dve.wait_ge(attn_made, c.times(1, 1))
                    take_moments("attn", c, attn_rows)
                if p == 3 and b.plus(-1).exists():
                    c = b.plus(-1)
                    dve.wait_ge(x1_made, c.times(1, 1))
                    take_moments("y", c, lambda t: x1[c.parity][:, t, :])
                if pair_exists(b, p + 1):
                    invert_sums(*batch_of(b, p + 1))
                if p == 2 and b.plus(-1).exists():
                    c = b.plus(-1)
                    wait(dve, x1_made, c.times(1, -1))
                    normalise("attn", c, attn_rows, attn_n[c.parity])
                if pair_exists(b, p - 1):
                    keep_heads(*batch_of(b, p - 1))
                if p == 3 and b.plus(-2).exists():
                    c = b.plus(-2)
                    dve.wait_ge(tanh_done, c.times(1, 1))
                    take_moments("ffn", c, lambda t: ffn_th[c.parity][:, t, :])

            all_slots(dve, slot, prepare)

        @block.tensor
        def _(pe_eng):
            mm = nc.tensor.matmul
            pe_eng.wait_ge(ready_dve, 1)
            mm(misc_bank[:, 0:P], w2_sb[:, :], w1t_sb[:, :], start=True, stop=True).then_inc(fused_pe, 1)
            pe_eng.wait_ge(fused_dve, 1)
            mm(misc_bank[:, P:2 * P], w12t_sb[:, :], w3_sb[:, :], start=True, stop=True)
            mm(misc_bank[:, 2 * P:3 * P], ones_row[:, :], bias_row[:, :], start=True, stop=True).then_inc(fused_pe, 1)
            pe_eng.wait_ge(ready_split, 3)
            pe_eng.wait_ge(fused_dve, 2)

            def make_vals(b, t):
                hi, lo = xt_hi[b.parity][:, t * P:(t + 1) * P], xt_lo[b.parity][:, t * P:(t + 1) * P]
                v = slice(2 * F, 3 * F)
                mm(misc_bank[:, :], hi, w_hi[:, v], start=True, stop=False)
                mm(misc_bank[:, :], hi, w_lo[:, v], start=False, stop=False)
                mm(misc_bank[:, :], lo, w_hi[:, v], start=False, stop=True).then_inc(vals_made, 1)

            def make_scores(b, p):
                i = p % 2
                pe_eng.wait_ge(qk_kept, pair(b, p + 1))
                wait(pe_eng, inv_kept, pair(b, p - 1))
                for q_lo, k_hi, at in ((P, T, 0), (0, P, T)):
                    for h in range(2):
                        r = slice(h * D, (h + 1) * D)
                        mm(s_bank[h][i][:, at:at + k_hi], qk[i][r, q_lo:q_lo + P], qk[i][r, T:T + k_hi],
                           start=(at == 0), stop=False)
                for h in range(2):
                    mm(s_bank[h][i][:, P:SC], ident_b[:, :], mask[:, :], start=False, stop=True
                       ).then_inc(scores_made, 1)

            def make_qk(b, p):
                pe_eng.wait_ge(x_lo_kept, b.times(1, 1))
                wait(pe_eng, qk_kept, pair(b, p))
                hi, lo = xt_hi[b.parity], xt_lo[b.parity]
                for part in range(2):
                    f = slice(part * F + p * P, part * F + (p + 1) * P)
                    to = qk_bank[:, part * T:(part + 1) * T]
                    mm(to, w_hi[:, f], hi[:, :], start=True, stop=False)
                    mm(to, w_hi[:, f], lo[:, :], start=False, stop=False)
                    ins = mm(to, w_lo[:, f], hi[:, :], start=False, stop=True)
                ins.then_inc(qk_made, 1)

            def make_heads(b, p):
                i = p % 2
                pe_eng.wait_ge(pt1_kept, pair(b, p + 1))
                pe_eng.wait_ge(pt0_kept, pair(b, p + 1))
                pe_eng.wait_ge(vals_kept, b.times(2, 2))
                wait(pe_eng, heads_kept, pair(b, p))
                for s, to, rhs in ((0, slice(T, 2 * T), pt0), (1, slice(T + P, 2 * T), pt1)):
                    for h in range(2):
                        f = (2 * p + h) * D
                        ins = mm(turn_out_bank[h * D:(h + 1) * D, to], vals[b.parity][:, s, f:f + D], rhs[i][:, h, :],
                                 start=(s == 0), stop=(s == 1))
                ins.then_inc(heads_made, 1)

            def turn_probs(b, p):
                i = p % 2
                pe_eng.wait_ge(exps_done, b.times(2 * PAIRS, 2 * p + 2))
                wait(pe_eng, pt0_kept, pair(b, p))
                for h in range(2):
                    ins = nc.tensor.transpose(turn_out_bank[:, h * P:(h + 1) * P], probs[i][:, h, P:T], ident[:, :])
                ins.then_inc(turned1, 1)
                for h in range(2):
                    nc.tensor.transpose(turn_bank[:, h, P:T], probs[i][:, h, 0:P], ident[:, :])
                    ins = nc.tensor.transpose(turn_bank[:, h, 0:P], probs[i][:, h, T:SC], ident[:, :])
                ins.then_inc(turned0, 1)

            def turn_inv(b, p):
                i = p % 2
                pe_eng.wait_ge(inv_spread, pair(b, p + 1))
                for j in range(TT):
                    every = inv_wide[i][:, j, :, :].rearrange("p h d -> p (h d)")
                    ins = nc.tensor.transpose(s_bank[j][i][:, SC:SC + P], every, ident[:, :])
                ins.then_inc(inv_turned, 1)

            def turn_rows(source, at, made):
                for t in range(TT):
                    ins = nc.tensor.transpose(misc_bank[:, at + t * P:at + (t + 1) * P], source[:, t, :], ident[:, :])
                ins.then_inc(made, 1)

            def slot(b, p):
                if pair_exists(b, p + 1):
                    make_scores(*batch_of(b, p + 1))
                if pair_exists(b, p):
                    turn_inv(b, p)
                if p == 0 and b.exists():
                    pe_eng.wait_ge(vals_kept, b.times(2, 1))
                    make_vals(b, 1)
                if pair_exists(b, p + 2):
                    make_qk(*batch_of(b, p + 2))
                if p == 3 and b.plus(1).exists():
                    c = b.plus(1)
                    pe_eng.wait_ge(x_lo_kept, c.times(1, 1))
                    wait(pe_eng, norms["attn"]["normed"], b.times(1))
                    wait(pe_eng, ffn_kept, b.times(1, -1))
                    make_vals(c, 0)
                if p == 1:
                    if b.plus(1).exists():
                        pe_eng.wait_ge(x_lo_kept, b.times(1, 2))
                    wait(pe_eng, y_kept, b.times(1, -1))
                if p == 1 and b.plus(-2).exists():
                    c = b.plus(-2)
                    for t in range(TT):
                        ins = mm(misc_bank[:, T + t * E:T + (t + 1) * E], yt[c.parity][:, t * P:(t + 1) * P], wf[:, :],
                                 start=True, stop=True)
                    ins.then_inc(ffn_made, 1)
                if p == 1 and b.plus(-1).exists():
                    c = b.plus(-1)
                    pe_eng.wait_ge(heads_kept, pair(b, 0))
                    for t in range(TT):
                        for k in range(PAIRS):
                            ins = mm(misc_bank[:, t * E:(t + 1) * E], heads_t[c.parity][:, k, t * P:(t + 1) * P],
                                     wo[:, k, :], start=(k == 0), stop=(k == PAIRS - 1))
                    ins.then_inc(attn_made, 1)
                if pair_exists(b, p - 1):
                    make_heads(*batch_of(b, p - 1))
                if pair_exists(b, p):
                    turn_probs(b, p)
                if p == 0 and b.plus(-2).exists():
                    c = b.plus(-2)
                    pe_eng.wait_ge(norms["y"]["normed"], c.times(1, 1))
                    if b.exists():
                        pe_eng.wait_ge(vals_kept, b.times(2, 2))
                    else:
                        pe_eng.wait_ge(ffn_kept, b.times(1, -2))
                    turn_rows(yn[c.parity], T, y_turned)
                if p == 0 and b.plus(1).exists():
                    c = b.plus(1)
                    pe_eng.wait_ge(norms["x"]["normed"], c.times(1, 1))
                    if b.exists():
                        pe_eng.wait_ge(vals_kept, b.times(2, 2))
                    turn_rows(xn[c.parity], 0, x_turned)

            all_slots(pe_eng, slot)


def kernel(L0_attn_x, L0_attn_Wqkv, L0_attn_Wo, L0_ffn_weight, L0_ffn_aux_weight1, L0_ffn_aux_weight2, L0_ffn_bias):
    import numpy as _np
    import concourse.bacc as _bacc
    from concourse import mybir as _mybir
    from concourse.bass_utils import run_bass_kernel_spmd as _run

    B, T, E = L0_attn_x.shape
    H = 8
    D = L0_attn_Wo.shape[1] // H
    w_qkv_t = _np.asarray(L0_attn_Wqkv).reshape(H, 3, D, E).transpose(3, 1, 0, 2).reshape(E, 3 * H * D)
    inputs = {
        "x": L0_attn_x,
        "w_qkv_t": w_qkv_t,
        "w_o_t": _np.asarray(L0_attn_Wo).T,
        "w1_t": _np.asarray(L0_ffn_weight).T,
        "w2": L0_ffn_aux_weight1,
        "w3": L0_ffn_aux_weight2,
        "bias": L0_ffn_bias,
    }
    nc = _bacc.Bacc("TRN2", target_bir_lowering=False, num_devices=1)
    arrays, args = {}, []
    for name, a in inputs.items():
        a = _np.ascontiguousarray(a)
        arrays[f"in_{name}"] = a
        args.append(nc.dram_tensor(f"in_{name}", a.shape, _mybir.dt.from_np(a.dtype), kind="ExternalInput").ap())
    out = nc.dram_tensor("out_x", (B, T, E), _mybir.dt.from_np(_np.dtype("float32")), kind="ExternalOutput").ap()
    build_block(nc, *args, out, H)
    r = _run(nc, [arrays], core_ids=[0])
    return r.results[0]["out_x"]
```
